# Optimizing a Trainium2 kernel written in Bass

```python
import numpy as np
import jax
import jax.numpy as jnp

def _softmax(x, axis=-1):
    return jax.nn.softmax(x, axis=axis)

def _gelu(x):
    return jax.nn.gelu(x, approximate=True)

def _silu(x):
    return jax.nn.silu(x)

def _sigmoid(x):
    return jax.nn.sigmoid(x)

def _layernorm(x, axis=-1, eps=1e-05):
    m = jnp.mean(x, axis=axis, keepdims=True)
    v = jnp.var(x, axis=axis, keepdims=True)
    return (x - m) / jnp.sqrt(v + eps)

def _scatter_add(tgt, idx, src, axis=0):
    return tgt.at[idx].add(src)

def _segment_sum(src, seg, n):
    return jax.ops.segment_sum(src, seg, n)
kernel_name = 'mk_cond_resid_d1_seqx_r4_0f8c7d'

def setup_inputs(seed: int=0):
    np.random.seed(seed)
    _w = jnp.asarray

    def _rec_inputs():
        import jax
        import jax.numpy as jnp
        _rk = jax.random.key(seed)
        x = 7.22e-05 + 1 * jax.random.normal(jax.random.fold_in(_rk, 1), (16, 256, 256), jnp.float32)
        _lenS = 256 - jax.random.randint(jax.random.fold_in(_rk, 7), (16,), 0, max(1, 256 // 4) + 1, jnp.int32)
        _lenS2 = 256 - jax.random.randint(jax.random.fold_in(_rk, 8), (16,), 0, max(1, 256 // 4) + 1, jnp.int32)
        fside_BxSxS_0 = 4.13588e-05 + 0.999923 * jax.random.normal(jax.random.fold_in(_rk, 11), (16, 256, 256), jnp.float32)
        itok_B_0_5 = jax.random.randint(jax.random.fold_in(_rk, 12), (16,), 0, 6, jnp.int32)
        return (x, fside_BxSxS_0, itok_B_0_5)
    x, fside_BxSxS_0, itok_B_0_5 = _rec_inputs()

    def _L0_cond_setup():
        import jax, jax.numpy as jnp
        import numpy as np
        B, S, D = (8, 256, 256)
        NUM_STAGES = 6
        key = jax.random.key(seed)
        k1, k2, k3, k4, k5 = jax.random.split(key, 5)
        return {'query': jax.random.normal(k1, (B, S, D), dtype=jnp.float32), 'key': jax.random.normal(k2, (B, S, D), dtype=jnp.float32), 'value': jax.random.normal(k3, (B, S, D), dtype=jnp.float32), 'braak_embed': jax.random.normal(k4, (NUM_STAGES, D), dtype=jnp.float32), 'braak_stages': jax.random.randint(k5, (B,), 0, NUM_STAGES, dtype=jnp.int64)}
    _L0_cond_all = _L0_cond_setup()
    _L0_cond_in = {k: v for k, v in _L0_cond_all.items() if k in ('braak_embed',)}
    del _L0_cond_all
    return {'x': x, 'fside_BxSxS_0': fside_BxSxS_0, 'itok_B_0_5': itok_B_0_5, 'L0_cond_braak_embed': _L0_cond_in['braak_embed']}

def reference(x, fside_BxSxS_0, itok_B_0_5, L0_cond_braak_embed):
    import jax
    import jax.numpy as jnp

    def _L0_cond_ref(query, key, value, braak_embed, braak_stages):
        import jax, jax.numpy as jnp
        import numpy as np
        B, S, D = (8, 256, 256)
        NUM_STAGES = 6
        bias = braak_embed[braak_stages][..., None]
        q = query + bias
        attn = jnp.einsum('bsd,btd->bst', q, key)
        attn = jax.nn.softmax(attn, axis=-1)
        return jnp.einsum('bst,btd->bsd', attn, value)
    x = x + _L0_cond_ref(x, fside_BxSxS_0, fside_BxSxS_0, L0_cond_braak_embed, itok_B_0_5)
    return x

_drawn_inputs = setup_inputs


def setup_inputs(seed=0):
    import zlib

    import numpy as np

    out = dict(_drawn_inputs(seed))
    spreads = {}
    factors = {}
    for name, (base, spread) in spreads.items():
        noise = np.random.default_rng([zlib.crc32(name.encode()), seed]).standard_normal(out[name].shape)
        drawn = base * np.exp(spread * noise) if base else spread * noise
        out[name] = jnp.asarray(drawn.astype(out[name].dtype))
    for name, factor in factors.items():
        out[name] = (out[name] * factor).astype(out[name].dtype)
    return out
```

```python
import concourse.bass as bass
from concourse import mybir
from contextlib import ExitStack


def attention_with_stage_bias(nc, x, fside, itok, embed, out):
    F32, F32R, I32 = mybir.dt.float32, mybir.dt.float32r, mybir.dt.int32
    ALU, ACT, AX = mybir.AluOpType, mybir.ActivationFunctionType, mybir.AxisListType

    P = 128
    B, S, D = x.shape
    STAGES = embed.shape[0]
    HALVES = S // P
    CHUNKS = D // P

    x_by_batch = x.rearrange("b (p h) d -> p b (h d)", h=HALVES)
    fside_by_batch = fside.rearrange("b (p h) d -> p b (h d)", h=HALVES)
    out_by_batch = out.rearrange("b (p h) d -> p b (h d)", h=HALVES)

    with ExitStack() as ctx:
        def sb(name, shape, dt=F32):
            return ctx.enter_context(nc.sbuf_tensor(name, shape, dt))

        def ps(name, shape, dt=F32):
            return ctx.enter_context(nc.psum_tensor(name, shape, dt))

        def sem(name):
            return ctx.enter_context(nc.semaphore(name))

        x_all = sb("x_all", [P, B, HALVES * D])
        v_hi = sb("v_hi", [P, B, HALVES * D], F32R)
        v_lo = sb("v_lo", [P, B, HALVES * D], F32R)
        k_nat = [sb(f"k_nat{i}", [P, HALVES, D]) for i in range(2)]
        q_nat = [sb(f"q_nat{i}", [P, HALVES, D]) for i in range(2)]
        qT_hi = [sb(f"qT_hi{i}", [P, CHUNKS, S], F32R) for i in range(2)]
        qT_lo = [sb(f"qT_lo{i}", [P, CHUNKS, S], F32R) for i in range(2)]
        kT_hi = [sb(f"kT_hi{i}", [P, CHUNKS, S], F32R) for i in range(2)]
        kT_lo = [sb(f"kT_lo{i}", [P, CHUNKS, S], F32R) for i in range(2)]
        probs = [sb(f"probs{i}", [P, HALVES, S]) for i in range(2)]
        pT_hi = [sb(f"pT_hi{i}", [P, HALVES, S], F32R) for i in range(2)]
        pT_lo = [sb(f"pT_lo{i}", [P, HALVES, S], F32R) for i in range(2)]
        result = [sb(f"result{i}", [P, HALVES, D]) for i in range(2)]
        negmax = [sb(f"negmax{i}", [P, HALVES]) for i in range(2)]
        rowsum = [sb(f"rowsum{i}", [P, HALVES]) for i in range(2)]
        recip = [sb(f"recip{i}", [P, HALVES]) for i in range(2)]
        ident = sb("ident", [P, P])
        embed_sb = sb("embed_sb", [STAGES, S])
        itok_i = sb("itok_i", [STAGES, B], I32)
        itok_f = sb("itok_f", [STAGES, B])
        stage_i = sb("stage_i", [STAGES, 1], I32)
        stage_f = sb("stage_f", [STAGES, 1])
        onehot = sb("onehot", [STAGES, B])
        bias = sb("bias", [P, B, HALVES])

        qT_ps = ps("qT_ps", [P, CHUNKS, S])
        kT_ps = [ps(f"kT_ps{i}", [P, CHUNKS, S]) for i in range(2)]
        pT_ps = ps("pT_ps", [P, HALVES, S])
        scores = [ps(f"scores{i}", [P, HALVES, S]) for i in range(2)]
        weighted = [ps(f"weighted{i}", [P, HALVES, D]) for i in range(2)]
        bias_ps = scores[0]

        x_loaded = [sem(f"x_loaded{i}") for i in range(2)]
        k_loaded = [sem(f"k_loaded{i}") for i in range(2)]
        stored = [sem(f"stored{i}") for i in range(2)]
        small_loaded = sem("small_loaded")
        ident_zeroed = sem("ident_zeroed")
        ident_ready = sem("ident_ready")
        stage_ready = sem("stage_ready")
        onehot_steps = sem("onehot_steps")
        bias_summed = sem("bias_summed")
        bias_ready = sem("bias_ready")
        q_ready = sem("q_ready")
        q_transposed = sem("q_transposed")
        k_transposed = sem("k_transposed")
        q_hi_ready = sem("q_hi_ready")
        q_lo_ready = sem("q_lo_ready")
        k_hi_ready = sem("k_hi_ready")
        k_lo_ready = sem("k_lo_ready")
        v_hi_ready = sem("v_hi_ready")
        v_lo_ready = sem("v_lo_ready")
        scores_ready = sem("scores_ready")
        max_ready = sem("max_ready")
        probs_ready = sem("probs_ready")
        p_transposed = sem("p_transposed")
        p_hi_ready = sem("p_hi_ready")
        p_lo_ready = sem("p_lo_ready")
        recip_ready = sem("recip_ready")
        weighted_ready = sem("weighted_ready")
        result_ready = sem("result_ready")

        block = ctx.enter_context(nc.Block())

        def transfers(b, slot):
            return (b - slot) * 8 + 16

        def steps(engine, step, first, last, loop_first, loop_last):
            for b in range(first, loop_first):
                step(b, b % 2)
            if LOOP:
                with engine.Fori(loop_first, loop_last, 2) as base:
                    for j in range(2):
                        step(base + j, (loop_first + j) % 2)
            for b in range(loop_last + 1 if LOOP else loop_first, last + 1):
                step(b, b % 2)

        def at_least(b, n):
            return not isinstance(b, int) or b >= n

        def below(b, n):
            return not isinstance(b, int) or b < n

        @block.sync
        def _(sp):
            def load(b, j):
                if at_least(b, 2):
                    sp.wait_ge(x_loaded[j], transfers(b - 2, j))
                sp.dma_start(x_all[:, b, :], x_by_batch[:, b, :]).then_inc(x_loaded[j], 16)
                if at_least(b, 2):
                    sp.wait_ge(k_transposed, b - 1)
                    sp.wait_ge(v_lo_ready, b - 1)
                sp.dma_start(k_nat[j][:, :, :].rearrange("p h d -> p (h d)"),
                             fside_by_batch[:, b, :]).then_inc(k_loaded[j], 16)

            def step(b, j):
                if below(b, B - 3):
                    load(b + 3, (j + 1) % 2)
                if at_least(b, 2):
                    sp.wait_ge(result_ready, b - 1)
                    sp.dma_start(out_by_batch[:, b - 2, :],
                                 result[j][:, :, :].rearrange("p h d -> p (h d)")
                                 ).then_inc(stored[j], 16)

            load(0, 0)
            sp.dma_start(embed_sb[:, :], embed).then_inc(small_loaded, 16)
            sp.dma_start(itok_i[:, :], itok.rearrange("(o b) -> o b", o=1).broadcast_to([STAGES, B])
                         ).then_inc(small_loaded, 16)
            load(1, 1)
            steps(sp, step, -1, B + 1, 2, B - 5)
            for slot in range(2):
                sp.wait_ge(stored[slot], 16 * B // 2)

        @block.gpsimd
        def _(pool):
            nc.gpsimd.iota(stage_i[:, :], [[0, 1]], base=0, channel_multiplier=1).then_inc(stage_ready, 1)
            nc.gpsimd.memset(ident[:, :], 0.0).then_inc(ident_zeroed, 1)
            pool.wait_ge(ident_zeroed, 1)
            nc.gpsimd.affine_select(out=ident[:, :], in_=ident[:, :], compare_op=ALU.not_equal, fill=1.0,
                                    base=0, pattern=[[-1, P]], channel_multiplier=1).then_inc(ident_ready, 1)
            pool.wait_ge(bias_ready, 1)

            def add_bias(b, j):
                pool.wait_ge(x_loaded[j], transfers(b, j))
                if at_least(b, 2):
                    pool.wait_ge(q_transposed, b - 1)
                nc.gpsimd.tensor_tensor(
                    q_nat[j][:, :, :], x_all[:, b, :].rearrange("p (h d) -> p h d", h=HALVES),
                    bias[:, b, :].rearrange("p (h o) -> p h o", o=1).broadcast_to([P, HALVES, D]), ALU.add).then_inc(q_ready, 1)

            def step(b, j):
                add_bias(b + 2, j)
                pool.wait_ge(v_hi_ready, b + 3)
                nc.gpsimd.tensor_tensor(v_lo[:, b + 2, :], k_nat[j][:, :, :].rearrange("p h d -> p (h d)"),
                                        v_hi[:, b + 2, :].bitcast(F32), ALU.subtract).then_inc(v_lo_ready, 1)

            steps(pool, step, -2, B - 3, 2, B - 3)

        @block.scalar
        def _(act):
            def step(b, j):
                if at_least(b, -1) and below(b, B - 1):
                    act.wait_ge(q_transposed, b + 2)
                    if at_least(b, 1):
                        act.wait_ge(scores_ready, b)
                    nc.scalar.copy(qT_hi[(j + 1) % 2][:, :, :], qT_ps[:, :, :]).then_inc(q_hi_ready, 1)
                if at_least(b, 1):
                    act.wait_ge(p_transposed, b)
                    if at_least(b, 3):
                        act.wait_ge(weighted_ready, b - 2)
                    nc.scalar.copy(pT_hi[(j + 1) % 2][:, :, :], pT_ps[:, :, :]).then_inc(p_hi_ready, 1)
                if at_least(b, -1) and below(b, B - 1):
                    act.wait_ge(k_transposed, b + 2)
                    nc.scalar.copy(kT_hi[(j + 1) % 2][:, :, :],
                                   kT_ps[(j + 1) % 2][:, :, :]).then_inc(k_hi_ready, 1)
                if below(b, B - 2):
                    act.wait_ge(k_loaded[j], transfers(b + 2, j))
                    nc.scalar.copy(v_hi[:, b + 2, :],
                                   k_nat[j][:, :, :].rearrange("p h d -> p (h d)")).then_inc(v_hi_ready, 1)
                if at_least(b, 0) and below(b, B):
                    act.wait_ge(max_ready, b + 1)
                    if at_least(b, 2):
                        act.wait_ge(p_transposed, b - 1)
                        act.wait_ge(recip_ready, b - 1)
                    for h in range(HALVES):
                        last = nc.scalar.activation(probs[j][:, h, :], scores[j][:, h, :], ACT.Exp,
                                                    bias=negmax[j][:, h:h + 1],
                                                    accum_out=rowsum[j][:, h:h + 1])
                    last.then_inc(probs_ready, 1)

            steps(act, step, -2, B, 3, B - 4)

        @block.vector
        def _(dve):
            dve.wait_ge(stage_ready, 1)
            nc.vector.tensor_copy(stage_f[:, :], stage_i[:, :])
            dve.wait_ge(small_loaded, 32)
            nc.vector.tensor_copy(itok_f[:, :], itok_i[:, :]).then_inc(onehot_steps, 1)
            dve.wait_ge(onehot_steps, 1)
            nc.vector.tensor_scalar(onehot[:, :], itok_f[:, :], stage_f[:, 0:1], None,
                                    ALU.is_equal).then_inc(onehot_steps, 1)
            dve.wait_ge(bias_summed, 1)
            nc.vector.tensor_copy(bias[:, :, :].rearrange("p b h -> p h b"),
                                  bias_ps[:, :, 0:B]).then_inc(bias_ready, 1)

            def step(b, j):
                if at_least(b, 2):
                    dve.wait_ge(weighted_ready, b - 1)
                    dve.wait_ge(recip_ready, b - 1)
                    if at_least(b, 4):
                        dve.wait_ge(stored[j], transfers(b - 4, j))
                    for h in range(HALVES):
                        last = nc.vector.scalar_tensor_tensor(
                            result[j][:, h, :], weighted[j][:, h, :], recip[j][:, h:h + 1],
                            x_all[:, b - 2, h * D:(h + 1) * D], ALU.mult, ALU.add)
                    last.then_inc(result_ready, 1)
                if below(b, B - 1):
                    dve.wait_ge(q_hi_ready, b + 2)
                    if at_least(b, 1):
                        dve.wait_ge(scores_ready, b)
                    nc.vector.tensor_tensor(qT_lo[(j + 1) % 2][:, :, :], qT_ps[:, :, :],
                                            qT_hi[(j + 1) % 2][:, :, :].bitcast(F32),
                                            ALU.subtract).then_inc(q_lo_ready, 1)
                if at_least(b, 1) and below(b, B + 1):
                    dve.wait_ge(p_hi_ready, b)
                    if at_least(b, 3):
                        dve.wait_ge(weighted_ready, b - 2)
                    nc.vector.tensor_tensor(pT_lo[(j + 1) % 2][:, :, :], pT_ps[:, :, :],
                                            pT_hi[(j + 1) % 2][:, :, :].bitcast(F32),
                                            ALU.subtract).then_inc(p_lo_ready, 1)
                    dve.wait_ge(probs_ready, b)
                    nc.vector.reciprocal(recip[(j + 1) % 2][:, :], rowsum[(j + 1) % 2][:, :]).then_inc(recip_ready, 1)
                if at_least(b, 0) and below(b, B):
                    dve.wait_ge(scores_ready, b + 1)
                    if at_least(b, 2):
                        dve.wait_ge(probs_ready, b - 1)
                    nc.vector.tensor_reduce(negmax[j][:, :], scores[j][:, :, :], axis=AX.X, op=ALU.max,
                                            negate=True).then_inc(max_ready, 1)
                if below(b, B - 1):
                    dve.wait_ge(k_hi_ready, b + 2)
                    nc.vector.tensor_tensor(kT_lo[(j + 1) % 2][:, :, :], kT_ps[(j + 1) % 2][:, :, :],
                                            kT_hi[(j + 1) % 2][:, :, :].bitcast(F32),
                                            ALU.subtract).then_inc(k_lo_ready, 1)

            steps(dve, step, -1, B + 1, 4, B - 3)

        @block.tensor
        def _(pe):
            pe.wait_ge(small_loaded, 32)
            pe.wait_ge(onehot_steps, 2)
            by_half = embed_sb[:, :].rearrange("g (p h) -> g h p", h=HALVES)
            for h in range(HALVES):
                last = nc.tensor.matmul(bias_ps[:, h, 0:B], by_half[:, h, :], onehot[:, :], start=True, stop=True)
            last.then_inc(bias_summed, 1)
            pe.wait_ge(ident_ready, 1)

            def transpose_halves(dst, src):
                for c in range(CHUNKS):
                    for h in range(HALVES):
                        last = nc.tensor.transpose(dst[:, c, h * P:(h + 1) * P],
                                                   src[:, h, c * P:(c + 1) * P], ident[:, :])
                return last

            def product(dst, left, right):
                for h in range(HALVES):
                    n = 0
                    for a, b in zip(left, right):
                        for c in range(CHUNKS):
                            last = nc.tensor.matmul(dst[:, h, :], a[:, c, h * P:(h + 1) * P], b[:, c, :],
                                                    start=n == 0, stop=n == len(left) * CHUNKS - 1)
                            n += 1
                return last

            def step(b, j):
                n = (j + 1) % 2
                if below(b, B - 1):
                    pe.wait_ge(q_ready, b + 2)
                    if at_least(b, 0):
                        pe.wait_ge(q_lo_ready, b + 1)
                    transpose_halves(qT_ps, q_nat[n]).then_inc(q_transposed, 1)
                    pe.wait_ge(k_loaded[n], transfers(b + 1, n))
                    if at_least(b, 1):
                        pe.wait_ge(k_lo_ready, b)
                    transpose_halves(kT_ps[n], k_nat[n]).then_inc(k_transposed, 1)
                if at_least(b, 1):
                    pe.wait_ge(probs_ready, b)
                    if at_least(b, 2):
                        pe.wait_ge(p_lo_ready, b - 1)
                    transpose_halves(pT_ps, probs[n]).then_inc(p_transposed, 1)
                if at_least(b, 0) and below(b, B):
                    pe.wait_ge(q_lo_ready, b + 1)
                    pe.wait_ge(k_lo_ready, b + 1)
                    if at_least(b, 2):
                        pe.wait_ge(probs_ready, b - 1)
                    elif b == 0:
                        pe.wait_ge(bias_ready, 1)
                    product(scores[j], [qT_hi[j], qT_lo[j], qT_hi[j]],
                            [kT_hi[j], kT_hi[j], kT_lo[j]]).then_inc(scores_ready, 1)
                if at_least(b, 1):
                    v_hi_b, v_lo_b = (v[:, b - 1, :].rearrange("p (h d) -> p h d", h=HALVES) for v in (v_hi, v_lo))
                    pe.wait_ge(v_lo_ready, b)
                    pe.wait_ge(p_lo_ready, b)
                    if at_least(b, 3):
                        pe.wait_ge(result_ready, b - 2)
                    product(weighted[n], [pT_hi[n], pT_hi[n], pT_lo[n]],
                            [v_hi_b, v_lo_b, v_hi_b]).then_inc(weighted_ready, 1)

            steps(pe, step, -1, B, 3, B - 2)


LOOP = True


_INS = ["x", "fside_BxSxS_0", "itok_B_0_5", "L0_cond_braak_embed"]


def kernel(**inputs):
    import numpy as _np
    import concourse.bacc as _bacc
    from concourse import mybir as _mybir
    from concourse.bass_utils import run_bass_kernel_spmd as _run

    nc = _bacc.Bacc("TRN2", target_bir_lowering=False, num_devices=1)
    arrays, args = {}, []
    for name in _INS:
        a = _np.ascontiguousarray(inputs[name])
        arrays[f"in_{name}_dram"] = a
        args.append(nc.dram_tensor(f"in_{name}_dram", a.shape, _mybir.dt.from_np(a.dtype), kind="ExternalInput").ap())
    out = nc.dram_tensor("out_dram", inputs["x"].shape, _mybir.dt.float32, kind="ExternalOutput").ap()
    attention_with_stage_bias(nc, *args, out)
    r = _run(nc, [arrays], core_ids=[0])
    return r.results[0]["out_dram"]
```

```python
import concourse.bass as bass
from concourse import mybir
from contextlib import ExitStack


def attention_with_stage_bias(nc, x, fside, itok, embed, out):
    F32, F32R, I32 = mybir.dt.float32, mybir.dt.float32r, mybir.dt.int32
    ALU, ACT, AX = mybir.AluOpType, mybir.ActivationFunctionType, mybir.AxisListType

    P = 128
    B, S, D = x.shape
    STAGES = embed.shape[0]
    HALVES = S // P
    CHUNKS = D // P

    x_by_batch = x.rearrange("b (p h) d -> p b (h d)", h=HALVES)
    fside_by_batch = fside.rearrange("b (p h) d -> p b (h d)", h=HALVES)
    out_by_batch = out.rearrange("b (p h) d -> p b (h d)", h=HALVES)

    with ExitStack() as ctx:
        def sb(name, shape, dt=F32):
            return ctx.enter_context(nc.sbuf_tensor(name, shape, dt))

        def ps(name, shape, dt=F32):
            return ctx.enter_context(nc.psum_tensor(name, shape, dt))

        def sem(name):
            return ctx.enter_context(nc.semaphore(name))

        x_all = sb("x_all", [P, B, HALVES * D])
        v_hi = sb("v_hi", [P, B, HALVES * D], F32R)
        v_lo = sb("v_lo", [P, B, HALVES * D], F32R)
        k_nat = [sb(f"k_nat{i}", [P, HALVES, D]) for i in range(2)]
        q_nat = [sb(f"q_nat{i}", [P, HALVES, D]) for i in range(2)]
        qT_hi = [sb(f"qT_hi{i}", [P, CHUNKS, S], F32R) for i in range(2)]
        qT_lo = [sb(f"qT_lo{i}", [P, CHUNKS, S], F32R) for i in range(2)]
        kT_hi = [sb(f"kT_hi{i}", [P, CHUNKS, S], F32R) for i in range(2)]
        kT_lo = [sb(f"kT_lo{i}", [P, CHUNKS, S], F32R) for i in range(2)]
        probs = [sb(f"probs{i}", [P, HALVES, S]) for i in range(2)]
        pT_hi = [sb(f"pT_hi{i}", [P, HALVES, S], F32R) for i in range(2)]
        pT_lo = [sb(f"pT_lo{i}", [P, HALVES, S], F32R) for i in range(2)]
        result = [sb(f"result{i}", [P, HALVES, D]) for i in range(2)]
        negmax = [sb(f"negmax{i}", [P, HALVES]) for i in range(2)]
        rowsum = [sb(f"rowsum{i}", [P, HALVES]) for i in range(2)]
        recip = [sb(f"recip{i}", [P, HALVES]) for i in range(2)]
        ident = sb("ident", [P, P])
        embed_sb = sb("embed_sb", [STAGES, S])
        itok_i = sb("itok_i", [STAGES, B], I32)
        itok_f = sb("itok_f", [STAGES, B])
        stage_i = sb("stage_i", [STAGES, 1], I32)
        stage_f = sb("stage_f", [STAGES, 1])
        onehot = sb("onehot", [STAGES, B])
        bias = sb("bias", [P, B, HALVES])

        qT_ps = ps("qT_ps", [P, CHUNKS, S])
        kT_ps = [ps(f"kT_ps{i}", [P, CHUNKS, S]) for i in range(2)]
        pT_ps = ps("pT_ps", [P, HALVES, S])
        scores = [ps(f"scores{i}", [P, HALVES, S]) for i in range(2)]
        weighted = [ps(f"weighted{i}", [P, HALVES, D]) for i in range(2)]
        bias_ps = scores[0]

        x_loaded = [sem(f"x_loaded{i}") for i in range(2)]
        k_loaded = [sem(f"k_loaded{i}") for i in range(2)]
        stored = [sem(f"stored{i}") for i in range(2)]
        small_loaded = sem("small_loaded")
        ident_zeroed = sem("ident_zeroed")
        ident_ready = sem("ident_ready")
        stage_ready = sem("stage_ready")
        onehot_steps = sem("onehot_steps")
        bias_summed = sem("bias_summed")
        bias_ready = sem("bias_ready")
        q_ready = sem("q_ready")
        q_transposed = sem("q_transposed")
        k_transposed = sem("k_transposed")
        q_hi_ready = sem("q_hi_ready")
        q_lo_ready = sem("q_lo_ready")
        k_hi_ready = sem("k_hi_ready")
        k_lo_ready = sem("k_lo_ready")
        v_hi_ready = sem("v_hi_ready")
        v_lo_ready = sem("v_lo_ready")
        scores_ready = sem("scores_ready")
        max_ready = sem("max_ready")
        probs_ready = sem("probs_ready")
        p_transposed = sem("p_transposed")
        p_hi_ready = sem("p_hi_ready")
        p_lo_ready = sem("p_lo_ready")
        recip_ready = sem("recip_ready")
        weighted_ready = sem("weighted_ready")
        result_ready = sem("result_ready")
        last_scores = sem("last_scores")
        last_max = sem("last_max")
        last_probs = sem("last_probs")
        last_transposed = sem("last_transposed")
        last_hi = sem("last_hi")
        last_lo = sem("last_lo")
        last_recip = sem("last_recip")
        last_weighted = sem("last_weighted")
        last_result = sem("last_result")

        LAST = B - 1
        last_s_ps = [scores[LAST % 2][:, 0, :], qT_ps[:, 0, :]]
        last_pT_ps = [kT_ps[0][:, :, 0:P], kT_ps[1][:, :, 0:P]]
        last_w_ps = [weighted[LAST % 2][:, 0, :], scores[(LAST + 1) % 2][:, 0, :]]

        block = ctx.enter_context(nc.Block())

        def landed(b, slot):
            return (b - slot) * 8 + 16

        def loop(engine, first, count, step):
            if LOOP:
                with engine.Fori(first, first + count - 1, 2) as b:
                    step(b, first % 2)
                    step(b + 1, (first + 1) % 2)
            else:
                for b in range(first, first + count):
                    step(b, b % 2)

        def after(b, n):
            return not isinstance(b, int) or b >= n

        def flat(tile):
            return tile.rearrange("p h d -> p (h d)")

        @block.sync
        def _(sp):
            def load_x(b, j):
                if after(b, 2):
                    sp.wait_ge(x_loaded[j], landed(b - 2, j))
                sp.dma_start(x_all[:, b, :], x_by_batch[:, b, :]).then_inc(x_loaded[j], 16)

            def load_k(b, j):
                if after(b, 2):
                    sp.wait_ge(k_transposed, b - 1)
                    sp.wait_ge(v_lo_ready, b - 1)
                sp.dma_start(flat(k_nat[j][:, :, :]), fside_by_batch[:, b, :]).then_inc(k_loaded[j], 16)

            def store(b, j):
                sp.wait_ge(result_ready, b + 1)
                sp.dma_start(out_by_batch[:, b, :], flat(result[j][:, :, :])).then_inc(stored[j], 16)

            def step(b, j):
                load_x(b + 3, 1 - j)
                load_k(b + 3, 1 - j)
                store(b - 2, j)

            sp.dma_start(itok_i[:, :], itok.rearrange("(o b) -> o b", o=1).broadcast_to([STAGES, B])
                         ).then_inc(small_loaded, 16)
            sp.dma_start(embed_sb[:, :], embed).then_inc(small_loaded, 16)
            load_k(0, 0)
            load_x(0, 0)
            load_k(1, 1)
            load_x(1, 1)
            for b in range(2, 5):
                load_x(b, b % 2)
                load_k(b, b % 2)
            loop(sp, 2, B - 6, step)
            for b in range(B - 4, B):
                if b + 3 < B:
                    load_x(b + 3, (b + 3) % 2)
                    load_k(b + 3, (b + 3) % 2)
                store(b - 2, b % 2)
            store(B - 2, B % 2)
            for h in range(HALVES):
                sp.wait_ge(last_result, h + 1)
                sp.dma_start(out_by_batch[:, LAST, h * D:(h + 1) * D],
                             result[LAST % 2][:, h, :]).then_inc(stored[LAST % 2], 16)
            sp.wait_ge(stored[B % 2], 16 * B // 2)
            sp.wait_ge(stored[LAST % 2], 16 * (B // 2 - 1 + HALVES))

        def bias_columns(b):
            return bias[:, b, :].rearrange("p (h o) -> p h o", o=1).broadcast_to([P, HALVES, D])

        @block.gpsimd
        def _(pool):
            nc.gpsimd.iota(stage_i[:, :], [[0, 1]], base=0, channel_multiplier=1).then_inc(stage_ready, 1)
            nc.gpsimd.memset(ident[:, :], 0.0).then_inc(ident_zeroed, 1)
            pool.wait_ge(ident_zeroed, 1)
            nc.gpsimd.affine_select(out=ident[:, :], in_=ident[:, :], compare_op=ALU.not_equal, fill=1.0,
                                    base=0, pattern=[[-1, P]], channel_multiplier=1).then_inc(ident_ready, 1)

            def add_bias(b, j):
                pool.wait_ge(x_loaded[j], landed(b, j))
                if after(b, 2):
                    pool.wait_ge(q_transposed, b - 1)
                nc.gpsimd.tensor_tensor(q_nat[j][:, :, :], x_all[:, b, :].rearrange("p (h d) -> p h d", h=HALVES),
                                        bias_columns(b), ALU.add).then_inc(q_ready, 1)

            def cut_v(b, j):
                pool.wait_ge(v_hi_ready, b + 1)
                nc.gpsimd.tensor_tensor(v_lo[:, b, :], flat(k_nat[j][:, :, :]), v_hi[:, b, :].bitcast(F32),
                                        ALU.subtract).then_inc(v_lo_ready, 1)

            def step(b, j):
                add_bias(b, j)
                cut_v(b, j)

            cut_v(0, 0)
            pool.wait_ge(bias_ready, 1)
            pool.wait_ge(q_ready, 1)
            step(1, 1)
            loop(pool, 2, B - 2, step)

        @block.scalar
        def _(act):
            def q_hi(b, j):
                act.wait_ge(q_transposed, b + 1)
                if after(b, 2):
                    act.wait_ge(scores_ready, b - 1)
                nc.scalar.copy(qT_hi[j][:, :, :], qT_ps[:, :, :]).then_inc(q_hi_ready, 1)

            def k_hi(b, j):
                act.wait_ge(k_transposed, b + 1)
                if after(b, 2):
                    act.wait_ge(scores_ready, b - 1)
                nc.scalar.copy(kT_hi[j][:, :, :], kT_ps[j][:, :, :]).then_inc(k_hi_ready, 1)

            def v_hi_of(b, j):
                act.wait_ge(k_loaded[j], landed(b, j))
                nc.scalar.copy(v_hi[:, b, :], flat(k_nat[j][:, :, :])).then_inc(v_hi_ready, 1)

            def p_hi(b, j):
                act.wait_ge(p_transposed, b + 1)
                if after(b, 2):
                    act.wait_ge(weighted_ready, b - 1)
                nc.scalar.copy(pT_hi[j][:, :, :], pT_ps[:, :, :]).then_inc(p_hi_ready, 1)

            def exp_half(h, src, j):
                return nc.scalar.activation(probs[j][:, h, :], src, ACT.Exp, bias=negmax[j][:, h:h + 1],
                                            accum_out=rowsum[j][:, h:h + 1])

            def exp(b, j):
                act.wait_ge(max_ready, b + 1)
                if after(b, 2):
                    act.wait_ge(p_transposed, b - 1)
                    act.wait_ge(recip_ready, b - 1)
                for h in range(HALVES):
                    last = exp_half(h, scores[j][:, h, :], j)
                last.then_inc(probs_ready, 1)

            def step(b, j):
                q_hi(b + 1, 1 - j)
                p_hi(b - 1, 1 - j)
                k_hi(b + 1, 1 - j)
                v_hi_of(b + 2, j)
                exp(b, j)

            v_hi_of(0, 0)
            k_hi(0, 0)
            q_hi(0, 0)
            v_hi_of(1, 1)
            k_hi(1, 1)
            q_hi(1, 1)
            v_hi_of(2, 0)
            exp(0, 0)
            p_hi(0, 0)
            k_hi(2, 0)
            q_hi(2, 0)
            v_hi_of(3, 1)
            exp(1, 1)
            step(2, 0)
            loop(act, 3, B - 6, step)
            step(B - 3, 1)
            q_hi(LAST, 1)
            p_hi(B - 3, 1)
            k_hi(LAST, 1)
            exp(B - 2, 0)
            p_hi(B - 2, 0)
            act.wait_ge(p_transposed, B - 2)
            act.wait_ge(recip_ready, B - 2)
            for h in range(HALVES):
                act.wait_ge(last_max, h + 1)
                exp_half(h, last_s_ps[h], LAST % 2).then_inc(last_probs, 1)
            act.wait_ge(weighted_ready, B - 2)
            for h in range(HALVES):
                act.wait_ge(last_transposed, h + 1)
                nc.scalar.copy(pT_hi[LAST % 2][:, :, h * P:(h + 1) * P], last_pT_ps[h]).then_inc(last_hi, 1)

        @block.vector
        def _(dve):
            dve.wait_ge(stage_ready, 1)
            nc.vector.tensor_copy(stage_f[:, :], stage_i[:, :])
            dve.wait_ge(small_loaded, 32)
            nc.vector.tensor_copy(itok_f[:, :], itok_i[:, :]).then_inc(onehot_steps, 1)
            dve.wait_ge(onehot_steps, 1)
            nc.vector.tensor_scalar(onehot[:, :], itok_f[:, :], stage_f[:, 0:1], None,
                                    ALU.is_equal).then_inc(onehot_steps, 1)
            dve.wait_ge(bias_summed, 1)
            nc.vector.tensor_copy(bias[:, :, :].rearrange("p b h -> p h b"),
                                  bias_ps[:, :, 0:B]).then_inc(bias_ready, 1)
            dve.wait_ge(bias_ready, 1)
            dve.wait_ge(x_loaded[0], landed(0, 0))
            nc.vector.tensor_tensor(q_nat[0][:, :, :], x_all[:, 0, :].rearrange("p (h d) -> p h d", h=HALVES),
                                    bias_columns(0), ALU.add).then_inc(q_ready, 1)

            def lo(dst, src, hi):
                return nc.vector.tensor_tensor(dst, src, hi.bitcast(F32), ALU.subtract)

            def q_lo(b, j):
                dve.wait_ge(q_hi_ready, b + 1)
                lo(qT_lo[j][:, :, :], qT_ps[:, :, :], qT_hi[j][:, :, :]).then_inc(q_lo_ready, 1)

            def k_lo(b, j):
                dve.wait_ge(k_hi_ready, b + 1)
                lo(kT_lo[j][:, :, :], kT_ps[j][:, :, :], kT_hi[j][:, :, :]).then_inc(k_lo_ready, 1)

            def p_lo(b, j):
                dve.wait_ge(p_hi_ready, b + 1)
                lo(pT_lo[j][:, :, :], pT_ps[:, :, :], pT_hi[j][:, :, :]).then_inc(p_lo_ready, 1)

            def reciprocal(b, j):
                dve.wait_ge(probs_ready, b + 1)
                nc.vector.reciprocal(recip[j][:, :], rowsum[j][:, :]).then_inc(recip_ready, 1)

            def maximum(b, j):
                dve.wait_ge(scores_ready, b + 1)
                nc.vector.tensor_reduce(negmax[j][:, :], scores[j][:, :, :], axis=AX.X, op=ALU.max,
                                        negate=True).then_inc(max_ready, 1)

            def finish_half(b, h, src, j):
                return nc.vector.scalar_tensor_tensor(result[j][:, h, :], src, recip[j][:, h:h + 1],
                                                      x_all[:, b, h * D:(h + 1) * D], ALU.mult, ALU.add)

            def finish(b, j):
                dve.wait_ge(weighted_ready, b + 1)
                dve.wait_ge(recip_ready, b + 1)
                if after(b, 2):
                    dve.wait_ge(stored[j], landed(b - 2, j))
                for h in range(HALVES):
                    last = finish_half(b, h, weighted[j][:, h, :], j)
                last.then_inc(result_ready, 1)

            def step(b, j):
                finish(b - 2, j)
                q_lo(b + 1, 1 - j)
                p_lo(b - 1, 1 - j)
                reciprocal(b - 1, 1 - j)
                maximum(b, j)
                k_lo(b + 1, 1 - j)

            k_lo(0, 0)
            q_lo(0, 0)
            k_lo(1, 1)
            maximum(0, 0)
            q_lo(1, 1)
            reciprocal(0, 0)
            maximum(1, 1)
            p_lo(0, 0)
            k_lo(2, 0)
            q_lo(2, 0)
            step(2, 0)
            step(3, 1)
            loop(dve, 4, B - 6, step)
            finish(B - 4, 0)
            q_lo(LAST, 1)
            p_lo(B - 3, 1)
            reciprocal(B - 3, 1)
            maximum(B - 2, 0)
            k_lo(LAST, 1)
            finish(B - 3, 1)
            p_lo(B - 2, 0)
            reciprocal(B - 2, 0)
            for h in range(HALVES):
                dve.wait_ge(last_scores, h + 1)
                nc.vector.tensor_reduce(negmax[LAST % 2][:, h:h + 1], last_s_ps[h], axis=AX.X, op=ALU.max,
                                        negate=True).then_inc(last_max, 1)
            dve.wait_ge(last_probs, HALVES)
            nc.vector.reciprocal(recip[LAST % 2][:, :], rowsum[LAST % 2][:, :]).then_inc(last_recip, 1)
            for h in range(HALVES):
                dve.wait_ge(last_hi, h + 1)
                lo(pT_lo[LAST % 2][:, :, h * P:(h + 1) * P], last_pT_ps[h],
                   pT_hi[LAST % 2][:, :, h * P:(h + 1) * P]).then_inc(last_lo, 1)
            finish(B - 2, 0)
            dve.wait_ge(last_recip, 1)
            dve.wait_ge(stored[LAST % 2], landed(LAST - 2, LAST % 2))
            for h in range(HALVES):
                dve.wait_ge(last_weighted, h + 1)
                finish_half(LAST, h, last_w_ps[h], LAST % 2).then_inc(last_result, 1)

        @block.tensor
        def _(pe):
            pe.wait_ge(small_loaded, 32)
            pe.wait_ge(onehot_steps, 2)
            by_half = embed_sb[:, :].rearrange("g (p h) -> g h p", h=HALVES)
            for h in range(HALVES):
                last = nc.tensor.matmul(bias_ps[:, h, 0:B], by_half[:, h, :], onehot[:, :], start=True, stop=True)
            last.then_inc(bias_summed, 1)
            pe.wait_ge(ident_ready, 1)

            def transpose(dst, src):
                for c in range(CHUNKS):
                    for h in range(HALVES):
                        last = nc.tensor.transpose(dst[:, c, h * P:(h + 1) * P],
                                                   src[:, h, c * P:(c + 1) * P], ident[:, :])
                return last

            def product(dst, h, terms, await_lo=()):
                for n, (left, right) in enumerate(terms):
                    if n and await_lo:
                        pe.wait_ge(*await_lo[n - 1])
                    for c in range(CHUNKS):
                        last = nc.tensor.matmul(dst, left[:, c, h * P:(h + 1) * P], right[:, c, :],
                                                start=n == 0 and c == 0, stop=n == 2 and c == CHUNKS - 1)
                return last

            def transpose_q(b, j):
                pe.wait_ge(q_ready, b + 1)
                if after(b, 1):
                    pe.wait_ge(q_lo_ready, b)
                transpose(qT_ps, q_nat[j]).then_inc(q_transposed, 1)

            def transpose_k(b, j):
                pe.wait_ge(k_loaded[j], landed(b, j))
                if after(b, 2):
                    pe.wait_ge(k_lo_ready, b - 1)
                transpose(kT_ps[j], k_nat[j]).then_inc(k_transposed, 1)

            def transpose_p(b, j):
                pe.wait_ge(probs_ready, b + 1)
                if after(b, 1):
                    pe.wait_ge(p_lo_ready, b)
                transpose(pT_ps, probs[j]).then_inc(p_transposed, 1)

            def score_terms(j):
                return [(qT_hi[j], kT_hi[j]), (qT_lo[j], kT_hi[j]), (qT_hi[j], kT_lo[j])]

            def score(b, j):
                pe.wait_ge(k_hi_ready, b + 1)
                pe.wait_ge(q_hi_ready, b + 1)
                if after(b, 2):
                    pe.wait_ge(probs_ready, b - 1)
                elif b == 0:
                    pe.wait_ge(bias_ready, 1)
                product(scores[j][:, 0, :], 0, score_terms(j), [(q_lo_ready, b + 1), (k_lo_ready, b + 1)])
                product(scores[j][:, 1, :], 1, score_terms(j)).then_inc(scores_ready, 1)

            def value_terms(b, j):
                hi, lo = (v[:, b, :].rearrange("p (h d) -> p h d", h=HALVES) for v in (v_hi, v_lo))
                return [(pT_hi[j], hi), (pT_hi[j], lo), (pT_lo[j], hi)]

            def weigh(b, j, half=None):
                if half != 1:
                    pe.wait_ge(p_hi_ready, b + 1)
                    if after(b, 2):
                        pe.wait_ge(result_ready, b - 1)
                    product(weighted[j][:, 0, :], 0, value_terms(b, j), [(v_lo_ready, b + 1), (p_lo_ready, b + 1)])
                if half != 0:
                    product(weighted[j][:, 1, :], 1, value_terms(b, j)).then_inc(weighted_ready, 1)

            def step(b, j):
                transpose_q(b + 1, 1 - j)
                transpose_k(b + 1, 1 - j)
                transpose_p(b - 1, 1 - j)
                score(b, j)
                weigh(b - 1, 1 - j)

            transpose_k(0, 0)
            transpose_q(0, 0)
            transpose_k(1, 1)
            score(0, 0)
            transpose_q(1, 1)
            score(1, 1)
            transpose_p(0, 0)
            transpose_k(2, 0)
            transpose_q(2, 0)
            weigh(0, 0)
            step(2, 0)
            loop(pe, 3, B - 4, step)
            transpose_p(B - 2, 0)
            pe.wait_ge(q_lo_ready, B)
            pe.wait_ge(k_lo_ready, B)
            pe.wait_ge(probs_ready, B - 2)
            for h in range(HALVES):
                product(last_s_ps[h], h, score_terms(LAST % 2)).then_inc(last_scores, 1)

            def transpose_last(h):
                pe.wait_ge(last_probs, h + 1)
                for c in range(CHUNKS):
                    last = nc.tensor.transpose(last_pT_ps[h][:, c, :],
                                               probs[LAST % 2][:, h, c * P:(c + 1) * P], ident[:, :])
                last.then_inc(last_transposed, 1)

            weigh(B - 2, 0, half=0)
            transpose_last(0)
            weigh(B - 2, 0, half=1)
            transpose_last(1)
            pe.wait_ge(result_ready, B - 2)
            pe.wait_ge(v_lo_ready, B)
            for h in range(HALVES):
                pe.wait_ge(last_hi, h + 1)
                product(last_w_ps[h], h, value_terms(LAST, LAST % 2),
                        [(v_lo_ready, B), (last_lo, h + 1)]).then_inc(last_weighted, 1)


LOOP = True


_INS = ["x", "fside_BxSxS_0", "itok_B_0_5", "L0_cond_braak_embed"]


def kernel(**inputs):
    import numpy as _np
    import concourse.bacc as _bacc
    from concourse import mybir as _mybir
    from concourse.bass_utils import run_bass_kernel_spmd as _run

    nc = _bacc.Bacc("TRN2", target_bir_lowering=False, num_devices=1)
    arrays, args = {}, []
    for name in _INS:
        a = _np.ascontiguousarray(inputs[name])
        arrays[f"in_{name}_dram"] = a
        args.append(nc.dram_tensor(f"in_{name}_dram", a.shape, _mybir.dt.from_np(a.dtype), kind="ExternalInput").ap())
    out = nc.dram_tensor("out_dram", inputs["x"].shape, _mybir.dt.float32, kind="ExternalOutput").ap()
    attention_with_stage_bias(nc, *args, out)
    r = _run(nc, [arrays], core_ids=[0])
    return r.results[0]["out_dram"]
```

```python
import concourse.bass as bass
from concourse import mybir
from contextlib import ExitStack


def attention_with_stage_bias(nc, x, fside, itok, embed, out):
    F32, F32R, I32 = mybir.dt.float32, mybir.dt.float32r, mybir.dt.int32
    ALU, ACT, AX = mybir.AluOpType, mybir.ActivationFunctionType, mybir.AxisListType

    P = 128
    B, S, D = x.shape
    STAGES = embed.shape[0]
    HALVES = S // P
    CHUNKS = D // P

    x_by_batch = x.rearrange("b (p h) d -> p b (h d)", h=HALVES)
    fside_by_batch = fside.rearrange("b (p h) d -> p b (h d)", h=HALVES)
    out_by_batch = out.rearrange("b (p h) d -> p b (h d)", h=HALVES)

    with ExitStack() as ctx:
        def sb(name, shape, dt=F32):
            return ctx.enter_context(nc.sbuf_tensor(name, shape, dt))

        def ps(name, shape, dt=F32):
            return ctx.enter_context(nc.psum_tensor(name, shape, dt))

        def sem(name):
            return ctx.enter_context(nc.semaphore(name))

        x_all = sb("x_all", [P, B, HALVES * D])
        v_hi = sb("v_hi", [P, B, HALVES * D], F32R)
        v_lo = sb("v_lo", [P, B, HALVES * D], F32R)
        k_nat = [sb(f"k_nat{i}", [P, HALVES, D]) for i in range(2)]
        first_k_nat = [sb(f"first_k_nat{i}", [P, HALVES, D]) for i in range(2)]
        q_nat = [sb(f"q_nat{i}", [P, HALVES, D]) for i in range(2)]
        qT_hi = [sb(f"qT_hi{i}", [P, CHUNKS, S], F32R) for i in range(2)]
        qT_lo = [sb(f"qT_lo{i}", [P, CHUNKS, S], F32R) for i in range(2)]
        kT_hi = [sb(f"kT_hi{i}", [P, CHUNKS, S], F32R) for i in range(2)]
        kT_lo = [sb(f"kT_lo{i}", [P, CHUNKS, S], F32R) for i in range(2)]
        probs = [sb(f"probs{i}", [P, HALVES, S]) for i in range(2)]
        pT_hi = [sb(f"pT_hi{i}", [P, HALVES, S], F32R) for i in range(2)]
        pT_lo = [sb(f"pT_lo{i}", [P, HALVES, S], F32R) for i in range(2)]
        result = [sb(f"result{i}", [P, HALVES, D]) for i in range(2)]
        negmax = [sb(f"negmax{i}", [P, HALVES]) for i in range(2)]
        rowsum = [sb(f"rowsum{i}", [P, HALVES]) for i in range(2)]
        recip = [sb(f"recip{i}", [P, HALVES]) for i in range(2)]
        ident = sb("ident", [P, P])
        warm_up = sb("warm_up", [P, 512], mybir.dt.bfloat16)
        embed_sb = sb("embed_sb", [STAGES, S])
        itok_i = sb("itok_i", [STAGES, B], I32)
        itok_f = sb("itok_f", [STAGES, B])
        stage_i = sb("stage_i", [STAGES, 1], I32)
        stage_f = sb("stage_f", [STAGES, 1])
        onehot = sb("onehot", [STAGES, B])
        bias = sb("bias", [P, B, HALVES])

        qT_ps = [ps(f"qT_ps{i}", [P, CHUNKS, S]) for i in range(2)]
        kT_ps = [ps(f"kT_ps{i}", [P, CHUNKS, S]) for i in range(2)]
        pT_ps = ps("pT_ps", [P, HALVES, S])
        scores = [ps(f"scores{i}", [P, HALVES, S]) for i in range(2)]
        weighted = ps("weighted", [P, HALVES, D])
        bias_ps = scores[0]

        x_loaded = [sem(f"x_loaded{i}") for i in range(2)]
        k_loaded = [sem(f"k_loaded{i}") for i in range(2)]
        stored = [sem(f"stored{i}") for i in range(2)]
        small_loaded = sem("small_loaded")
        warm_up_ready = sem("warm_up_ready")
        ident_zeroed = sem("ident_zeroed")
        ident_ready = sem("ident_ready")
        stage_ready = sem("stage_ready")
        onehot_steps = sem("onehot_steps")
        bias_summed = sem("bias_summed")
        bias_ready = sem("bias_ready")
        q_ready = sem("q_ready")
        q_transposed = sem("q_transposed")
        k_transposed = sem("k_transposed")
        q_hi_ready = sem("q_hi_ready")
        q_lo_ready = sem("q_lo_ready")
        k_hi_ready = sem("k_hi_ready")
        k_lo_ready = sem("k_lo_ready")
        v_hi_ready = sem("v_hi_ready")
        v_lo_ready = sem("v_lo_ready")
        scores_ready = sem("scores_ready")
        max_ready = sem("max_ready")
        probs_ready = sem("probs_ready")
        p_transposed = sem("p_transposed")
        p_hi_ready = sem("p_hi_ready")
        p_lo_ready = sem("p_lo_ready")
        recip_ready = sem("recip_ready")
        weighted_ready = sem("weighted_ready")
        result_ready = sem("result_ready")
        first_bias_added = sem("first_bias_added")
        first_transposed = sem("first_transposed")
        first_hi = sem("first_hi")
        first_lo = sem("first_lo")
        half_weighted = sem("half_weighted")
        last_scores = sem("last_scores")
        last_max = sem("last_max")
        last_probs = sem("last_probs")
        last_transposed = sem("last_transposed")
        last_hi = sem("last_hi")
        last_lo = sem("last_lo")
        last_recip = sem("last_recip")
        last_weighted = sem("last_weighted")
        last_result = sem("last_result")

        LAST = B - 1
        first_qT_ps = [qT_ps[0], pT_ps]
        early_w_ps = [weighted[:, 0, :], kT_ps[0][:, 0, :]]
        late_w_ps = [weighted[:, 0, :], scores[B % 2][:, 0, :]]
        last_s_ps = [scores[LAST % 2][:, 0, :], qT_ps[0][:, 0, :]]
        last_pT_ps = [kT_ps[0][:, :, 0:P], kT_ps[1][:, :, 0:P]]
        last_w_ps = [pT_ps[:, 0, :], qT_ps[1][:, 0, :]]
        second_w_ps = scores[1]

        block = ctx.enter_context(nc.Block())

        def landed(b, slot):
            return (b - slot) * 8 + 16

        def loop(engine, first, count, step):
            with engine.Fori(first, first + count - 1, 2) as b:
                step(b, first % 2)
                step(b + 1, (first + 1) % 2)

        def after(b, n):
            return not isinstance(b, int) or b >= n

        def k_of(b, j):
            return (k_nat if after(b, 2) else first_k_nat)[j][:, :, :]

        def flat(tile):
            return tile.rearrange("p h d -> p (h d)")

        @block.sync
        def _(sp):
            def load_x(b, j):
                if after(b, 2):
                    sp.wait_ge(x_loaded[j], landed(b - 2, j))
                sp.dma_start(x_all[:, b, :], x_by_batch[:, b, :]).then_inc(x_loaded[j], 16)

            def load_k(b, j):
                if after(b, 4):
                    sp.wait_ge(k_transposed, b - 1)
                    sp.wait_ge(v_lo_ready, b - 1)
                elif after(b, 2):
                    sp.wait_ge(k_loaded[j], landed(b - 2, j))
                sp.dma_start(flat(k_of(b, j)), fside_by_batch[:, b, :]).then_inc(k_loaded[j], 16)

            def store(b, j):
                sp.wait_ge(result_ready, b + 1)
                sp.dma_start(out_by_batch[:, b, :], flat(result[j][:, :, :])).then_inc(stored[j], 16)

            def step(b, j):
                load_x(b + 3, 1 - j)
                load_k(b + 3, 1 - j)
                store(b - 2, j)

            sp.dma_start(itok_i[:, :], itok.rearrange("(o b) -> o b", o=1).broadcast_to([STAGES, B])
                         ).then_inc(small_loaded, 16)
            sp.dma_start(embed_sb[:, :], embed).then_inc(small_loaded, 16)
            load_k(0, 0)
            load_x(0, 0)
            load_x(1, 1)
            load_k(1, 1)
            for b in range(2, 5):
                load_k(b, b % 2)
                load_x(b, b % 2)
            loop(sp, 2, B - 6, step)
            for b in range(B - 4, B):
                if b + 3 < B:
                    load_x(b + 3, (b + 3) % 2)
                    load_k(b + 3, (b + 3) % 2)
                store(b - 2, b % 2)
            for b in (B - 2, LAST):
                for h in range(HALVES):
                    sp.wait_ge(last_result, (b - (B - 2)) * HALVES + h + 1)
                    sp.dma_start(out_by_batch[:, b, h * D:(h + 1) * D],
                                 result[b % 2][:, h, :]).then_inc(stored[b % 2], 16)
            for slot in stored:
                sp.wait_ge(slot, 16 * (B // 2 - 1 + HALVES))

        def bias_columns(b):
            return bias[:, b, :].rearrange("p (h o) -> p h o", o=1).broadcast_to([P, HALVES, D])

        @block.gpsimd
        def _(pool):
            nc.gpsimd.iota(stage_i[:, :], [[0, 1]], base=0, channel_multiplier=1).then_inc(stage_ready, 1)
            nc.gpsimd.memset(ident[:, :], 0.0).then_inc(ident_zeroed, 1)
            pool.wait_ge(ident_zeroed, 1)
            nc.gpsimd.affine_select(out=ident[:, :], in_=ident[:, :], compare_op=ALU.not_equal, fill=1.0,
                                    base=0, pattern=[[-1, P]], channel_multiplier=1).then_inc(ident_ready, 1)

            def add_bias(b, j):
                pool.wait_ge(x_loaded[j], landed(b, j))
                if after(b, 2):
                    pool.wait_ge(q_transposed, b - 1)
                nc.gpsimd.tensor_tensor(q_nat[j][:, :, :], x_all[:, b, :].rearrange("p (h d) -> p h d", h=HALVES),
                                        bias_columns(b), ALU.add).then_inc(q_ready, 1)

            def cut_v(b, j):
                pool.wait_ge(v_hi_ready, b + 1)
                nc.gpsimd.tensor_tensor(v_lo[:, b, :], flat(k_of(b, j)), v_hi[:, b, :].bitcast(F32),
                                        ALU.subtract).then_inc(v_lo_ready, 1)

            def step(b, j):
                add_bias(b, j)
                cut_v(b, j)

            pool.wait_ge(bias_ready, 1)
            pool.wait_ge(q_ready, 1)
            add_bias(1, 1)
            pool.wait_ge(v_lo_ready, 1)
            cut_v(1, 1)
            add_bias(2, 0)
            add_bias(3, 1)
            cut_v(2, 0)
            cut_v(3, 1)
            add_bias(4, 0)
            cut_v(4, 0)
            step(5, 1)
            loop(pool, 6, B - 6, step)

        @block.scalar
        def _(act):
            def q_hi(b, j):
                act.wait_ge(q_transposed, b + 1)
                if after(b, 2):
                    act.wait_ge(scores_ready, b - 1)
                nc.scalar.copy(qT_hi[j][:, :, :], qT_ps[j][:, :, :]).then_inc(q_hi_ready, 1)

            def k_hi(b, j):
                act.wait_ge(k_transposed, b + 1)
                if after(b, 2):
                    act.wait_ge(scores_ready, b - 1)
                nc.scalar.copy(kT_hi[j][:, :, :], kT_ps[j][:, :, :]).then_inc(k_hi_ready, 1)

            def v_hi_of(b, j):
                act.wait_ge(k_loaded[j], landed(b, j))
                nc.scalar.copy(v_hi[:, b, :], flat(k_of(b, j))).then_inc(v_hi_ready, 1)

            def p_hi(b, j):
                act.wait_ge(p_transposed, b + 1)
                if after(b, 2):
                    act.wait_ge(weighted_ready, b - 1)
                nc.scalar.copy(pT_hi[j][:, :, :], pT_ps[:, :, :]).then_inc(p_hi_ready, 1)

            def exp_half(h, src, j):
                return nc.scalar.activation(probs[j][:, h, :], src, ACT.Exp, bias=negmax[j][:, h:h + 1],
                                            accum_out=rowsum[j][:, h:h + 1])

            def exp(b, j):
                act.wait_ge(max_ready, b + 1)
                if after(b, 2):
                    act.wait_ge(p_transposed, b - 1)
                    act.wait_ge(recip_ready, b - 1)
                for h in range(HALVES):
                    last = exp_half(h, scores[j][:, h, :], j)
                last.then_inc(probs_ready, 1)

            def step(b, j):
                q_hi(b + 1, 1 - j)
                p_hi(b - 1, 1 - j)
                k_hi(b + 1, 1 - j)
                v_hi_of(b + 2, j)
                exp(b, j)

            v_hi_of(0, 0)
            k_hi(0, 0)
            for h in range(HALVES):
                act.wait_ge((first_transposed, q_transposed)[h], 1)
                nc.scalar.copy(qT_hi[0][:, :, h * P:(h + 1) * P],
                               first_qT_ps[h][:, :, 0:P]).then_inc((first_hi, q_hi_ready)[h], 1)
            v_hi_of(1, 1)
            k_hi(1, 1)
            q_hi(1, 1)
            v_hi_of(2, 0)
            k_hi(2, 0)
            exp(0, 0)
            q_hi(2, 0)
            p_hi(0, 0)
            v_hi_of(3, 1)
            exp(1, 1)
            p_hi(1, 1)
            exp(2, 0)
            q_hi(3, 1)
            k_hi(3, 1)
            v_hi_of(4, 0)
            q_hi(4, 0)
            p_hi(2, 0)
            k_hi(4, 0)
            exp(3, 1)
            v_hi_of(5, 1)
            loop(act, 4, B - 6, step)
            q_hi(LAST, 1)
            p_hi(B - 3, 1)
            k_hi(LAST, 1)
            exp(B - 2, 0)
            act.wait_ge(p_transposed, B - 2)
            act.wait_ge(recip_ready, B - 2)
            p_hi(B - 2, 0)
            act.wait_ge(last_max, 1)
            exp_half(0, last_s_ps[0], LAST % 2).then_inc(last_probs, 1)
            act.wait_ge(last_max, 2)
            exp_half(1, last_s_ps[1], LAST % 2).then_inc(last_probs, 1)
            act.wait_ge(weighted_ready, B - 2)
            for h in range(HALVES):
                act.wait_ge(last_transposed, h + 1)
                nc.scalar.copy(pT_hi[LAST % 2][:, :, h * P:(h + 1) * P], last_pT_ps[h]).then_inc(last_hi, 1)

        @block.vector
        def _(dve):
            nc.vector.memset(warm_up[:, :], 0.0).then_inc(warm_up_ready, 1)
            dve.wait_ge(stage_ready, 1)
            nc.vector.tensor_copy(stage_f[:, :], stage_i[:, :])
            dve.wait_ge(small_loaded, 32)
            nc.vector.tensor_copy(itok_f[:, :], itok_i[:, :]).then_inc(onehot_steps, 1)
            dve.wait_ge(onehot_steps, 1)
            nc.vector.tensor_scalar(onehot[:, :], itok_f[:, :], stage_f[:, 0:1], None,
                                    ALU.is_equal).then_inc(onehot_steps, 1)
            dve.wait_ge(bias_summed, 1)
            nc.vector.tensor_copy(bias[:, :, :].rearrange("p b h -> p h b"),
                                  bias_ps[:, :, 0:B]).then_inc(bias_ready, 1)
            dve.wait_ge(bias_ready, 1)
            dve.wait_ge(x_loaded[0], landed(0, 0))
            for h in range(HALVES):
                nc.vector.tensor_scalar(q_nat[0][:, h, :], x_all[:, 0, h * D:(h + 1) * D], bias[:, 0, h:h + 1],
                                        None, ALU.add).then_inc((first_bias_added, q_ready)[h], 1)

            def lo(dst, src, hi):
                return nc.vector.tensor_tensor(dst, src, hi.bitcast(F32), ALU.subtract)

            def q_lo(b, j):
                dve.wait_ge(q_hi_ready, b + 1)
                lo(qT_lo[j][:, :, :], qT_ps[j][:, :, :], qT_hi[j][:, :, :]).then_inc(q_lo_ready, 1)

            def k_lo(b, j):
                dve.wait_ge(k_hi_ready, b + 1)
                lo(kT_lo[j][:, :, :], kT_ps[j][:, :, :], kT_hi[j][:, :, :]).then_inc(k_lo_ready, 1)

            def p_lo(b, j):
                dve.wait_ge(p_hi_ready, b + 1)
                lo(pT_lo[j][:, :, :], pT_ps[:, :, :], pT_hi[j][:, :, :]).then_inc(p_lo_ready, 1)

            def reciprocal(b, j):
                dve.wait_ge(probs_ready, b + 1)
                nc.vector.reciprocal(recip[j][:, :], rowsum[j][:, :]).then_inc(recip_ready, 1)

            def maximum(b, j):
                dve.wait_ge(scores_ready, b + 1)
                nc.vector.tensor_reduce(negmax[j][:, :], scores[j][:, :, :], axis=AX.X, op=ALU.max,
                                        negate=True).then_inc(max_ready, 1)

            def finish_half(b, h, src, j):
                return nc.vector.scalar_tensor_tensor(result[j][:, h, :], src, recip[j][:, h:h + 1],
                                                      x_all[:, b, h * D:(h + 1) * D], ALU.mult, ALU.add)

            def finish(b, j, src=weighted):
                dve.wait_ge(weighted_ready, b + 1)
                dve.wait_ge(recip_ready, b + 1)
                if after(b, 2):
                    dve.wait_ge(stored[j], landed(b - 2, j))
                for h in range(HALVES):
                    last = finish_half(b, h, src[:, h, :], j)
                last.then_inc(result_ready, 1)

            def step(b, j):
                finish(b - 2, j)
                q_lo(b + 1, 1 - j)
                p_lo(b - 1, 1 - j)
                reciprocal(b - 1, 1 - j)
                maximum(b, j)
                k_lo(b + 1, 1 - j)

            dve.wait_ge(v_hi_ready, 1)
            lo(v_lo[:, 0, :], flat(k_of(0, 0)), v_hi[:, 0, :]).then_inc(v_lo_ready, 1)
            k_lo(0, 0)
            for h in range(HALVES):
                dve.wait_ge((first_hi, q_hi_ready)[h], 1)
                lo(qT_lo[0][:, :, h * P:(h + 1) * P], first_qT_ps[h][:, :, 0:P],
                   qT_hi[0][:, :, h * P:(h + 1) * P]).then_inc((first_lo, q_lo_ready)[h], 1)
            k_lo(1, 1)
            q_lo(1, 1)
            maximum(0, 0)
            k_lo(2, 0)
            q_lo(2, 0)
            maximum(1, 1)
            p_lo(0, 0)
            reciprocal(0, 0)
            maximum(2, 0)
            p_lo(1, 1)
            reciprocal(1, 1)
            finish(0, 0)
            q_lo(3, 1)
            finish(1, 1, second_w_ps)
            k_lo(3, 1)
            q_lo(4, 0)
            p_lo(2, 0)
            dve.wait_ge(result_ready, 1)
            reciprocal(2, 0)
            maximum(3, 1)
            k_lo(4, 0)
            loop(dve, 4, B - 6, step)
            finish(B - 4, 0)
            q_lo(LAST, 1)
            p_lo(B - 3, 1)
            reciprocal(B - 3, 1)
            maximum(B - 2, 0)
            k_lo(LAST, 1)

            def finish_by_halves(b, h, src, j):
                if h == 0:
                    dve.wait_ge(half_weighted, b - (B - 3) + 1)
                    dve.wait_ge(recip_ready, b + 1)
                    dve.wait_ge(stored[j], landed(b - 2, j))
                else:
                    dve.wait_ge(weighted_ready, b + 1)
                done = finish_half(b, h, src, j)
                if b == B - 2:
                    done.then_inc(last_result, 1)
                elif h == 1:
                    done.then_inc(result_ready, 1)

            def last_maximum(h):
                dve.wait_ge(last_scores, h + 1)
                nc.vector.tensor_reduce(negmax[LAST % 2][:, h:h + 1], last_s_ps[h], axis=AX.X, op=ALU.max,
                                        negate=True).then_inc(last_max, 1)

            def last_p_lo(h):
                dve.wait_ge(last_hi, h + 1)
                lo(pT_lo[LAST % 2][:, :, h * P:(h + 1) * P], last_pT_ps[h],
                   pT_hi[LAST % 2][:, :, h * P:(h + 1) * P]).then_inc(last_lo, 1)

            finish_by_halves(B - 3, 0, early_w_ps[0], 1)
            last_maximum(0)
            finish_by_halves(B - 3, 1, early_w_ps[1], 1)
            last_maximum(1)
            p_lo(B - 2, 0)
            reciprocal(B - 2, 0)
            dve.wait_ge(last_probs, HALVES)
            nc.vector.reciprocal(recip[LAST % 2][:, :], rowsum[LAST % 2][:, :]).then_inc(last_recip, 1)
            last_p_lo(0)
            finish_by_halves(B - 2, 0, late_w_ps[0], 0)
            last_p_lo(1)
            finish_by_halves(B - 2, 1, late_w_ps[1], 0)
            dve.wait_ge(last_recip, 1)
            dve.wait_ge(stored[LAST % 2], landed(LAST - 2, LAST % 2))
            for h in range(HALVES):
                dve.wait_ge(last_weighted, h + 1)
                finish_half(LAST, h, last_w_ps[h], LAST % 2).then_inc(last_result, 1)

        @block.tensor
        def _(pe):
            def keep_clock_up(count, columns):
                for _ in range(count):
                    nc.tensor.matmul(weighted[:, :, :].rearrange("p h d -> p (h d)")[:, 0:columns],
                                     warm_up[:, 0:P], warm_up[:, 0:columns], start=True, stop=True)

            pe.wait_ge(warm_up_ready, 1)
            keep_clock_up(7, 512)
            pe.wait_ge(small_loaded, 32)
            pe.wait_ge(onehot_steps, 2)
            by_half = embed_sb[:, :].rearrange("g (p h) -> g h p", h=HALVES)
            for h in range(HALVES):
                last = nc.tensor.matmul(bias_ps[:, h, 0:B], by_half[:, h, :], onehot[:, :], start=True, stop=True)
            last.then_inc(bias_summed, 1)
            pe.wait_ge(ident_ready, 1)

            def transpose(dst, src):
                for c in range(CHUNKS):
                    for h in range(HALVES):
                        last = nc.tensor.transpose(dst[:, c, h * P:(h + 1) * P],
                                                   src[:, h, c * P:(c + 1) * P], ident[:, :])
                return last

            def product(dst, h, terms, await_lo=(), part=range(3)):
                for n in part:
                    left, right = terms[n]
                    if n and await_lo:
                        pe.wait_ge(*await_lo[n - 1])
                    for c in range(CHUNKS):
                        last = nc.tensor.matmul(dst, left[:, c, h * P:(h + 1) * P], right[:, c, :],
                                                start=n == 0 and c == 0, stop=n == 2 and c == CHUNKS - 1)
                return last

            def transpose_q(b, j):
                pe.wait_ge(q_ready, b + 1)
                if after(b, 2):
                    pe.wait_ge(q_lo_ready, b - 1)
                transpose(qT_ps[j], q_nat[j]).then_inc(q_transposed, 1)

            def transpose_k(b, j):
                pe.wait_ge(k_loaded[j], landed(b, j))
                if after(b, 2):
                    pe.wait_ge(k_lo_ready, b - 1)
                transpose(kT_ps[j], k_of(b, j)).then_inc(k_transposed, 1)

            def transpose_p(b, j):
                pe.wait_ge(probs_ready, b + 1)
                if after(b, 1):
                    pe.wait_ge(p_lo_ready, b)
                else:
                    pe.wait_ge(q_lo_ready, 1)
                transpose(pT_ps, probs[j]).then_inc(p_transposed, 1)

            def score_terms(j):
                return [(qT_hi[j], kT_hi[j]), (qT_lo[j], kT_hi[j]), (qT_hi[j], kT_lo[j])]

            def score(b, j, order=(0, 1, 2), between=lambda: None):
                pe.wait_ge(k_hi_ready, b + 1)
                pe.wait_ge(q_hi_ready, b + 1)
                if after(b, 2):
                    pe.wait_ge(probs_ready, b - 1)
                lo_ready = [None, (q_lo_ready, b + 1), (k_lo_ready, b + 1)]
                terms = [score_terms(j)[n] for n in order]
                product(scores[j][:, 0, :], 0, terms, [lo_ready[n] for n in order[1:]])
                between()
                product(scores[j][:, 1, :], 1, terms).then_inc(scores_ready, 1)

            def value_terms(b, j):
                hi, lo = (v[:, b, :].rearrange("p (h d) -> p h d", h=HALVES) for v in (v_hi, v_lo))
                return [(pT_hi[j], hi), (pT_hi[j], lo), (pT_lo[j], hi)]

            def await_weigh(b):
                pe.wait_ge(p_hi_ready, b + 1)
                if after(b, 1):
                    pe.wait_ge(result_ready, b)

            def weigh(b, j, between=lambda: None):
                await_weigh(b)
                product(weighted[:, 0, :], 0, value_terms(b, j), [(v_lo_ready, b + 1), (p_lo_ready, b + 1)])
                between()
                product(weighted[:, 1, :], 1, value_terms(b, j)).then_inc(weighted_ready, 1)

            def step(b, j):
                transpose_q(b + 1, 1 - j)
                transpose_k(b + 1, 1 - j)
                transpose_p(b - 1, 1 - j)
                score(b, j)
                weigh(b - 1, 1 - j)

            def transpose_last(h):
                pe.wait_ge(last_probs, h + 1)
                for c in range(CHUNKS):
                    last = nc.tensor.transpose(last_pT_ps[h][:, c, :],
                                               probs[LAST % 2][:, h, c * P:(c + 1) * P], ident[:, :])
                last.then_inc(last_transposed, 1)

            transpose_k(0, 0)
            for h in range(HALVES):
                pe.wait_ge((first_bias_added, q_ready)[h], 1)
                for c in range(CHUNKS):
                    last = nc.tensor.transpose(first_qT_ps[h][:, c, 0:P],
                                               q_nat[0][:, h, c * P:(c + 1) * P], ident[:, :])
                last.then_inc((first_transposed, q_transposed)[h], 1)
            transpose_k(1, 1)
            pe.wait_ge(bias_ready, 1)
            pe.wait_ge(k_hi_ready, 1)
            pe.wait_ge(first_hi, 1)
            product(scores[0][:, 0, :], 0, score_terms(0), part=range(1))
            transpose_q(1, 1)
            product(scores[0][:, 0, :], 0, score_terms(0), [(first_lo, 1), (k_lo_ready, 1)], part=range(1, 3))
            pe.wait_ge(q_hi_ready, 1)
            product(scores[0][:, 1, :], 1, score_terms(0), [(q_lo_ready, 1), (k_lo_ready, 1)]).then_inc(scores_ready, 1)

            k_lo_first = (0, 2, 1)
            transpose_k(2, 0)
            score(1, 1, k_lo_first, between=lambda: transpose_q(2, 0))
            transpose_p(0, 0)
            score(2, 0, k_lo_first)
            weigh(0, 0, between=lambda: transpose_p(1, 1))
            transpose_q(3, 1)
            transpose_k(3, 1)
            pe.wait_ge(p_hi_ready, 2)
            pe.wait_ge(probs_ready, 2)
            product(second_w_ps[:, 0, :], 0, value_terms(1, 1), [(v_lo_ready, 2), (p_lo_ready, 2)])
            product(second_w_ps[:, 1, :], 1, value_terms(1, 1)).then_inc(weighted_ready, 1)
            transpose_q(4, 0)
            transpose_k(4, 0)
            transpose_p(2, 0)
            pe.wait_ge(result_ready, 2)
            score(3, 1)
            weigh(2, 0)
            loop(pe, 4, B - 6, step)
            transpose_q(LAST, 1)
            transpose_k(LAST, 1)
            transpose_p(B - 3, 1)
            score(B - 2, 0)
            await_weigh(B - 3)
            await_lo = [(v_lo_ready, B - 2), (p_lo_ready, B - 2)]
            product(early_w_ps[0], 0, value_terms(B - 3, 1), await_lo).then_inc(half_weighted, 1)
            last_await_lo = [(q_lo_ready, B), (k_lo_ready, B)]
            pe.wait_ge(q_hi_ready, B)
            pe.wait_ge(k_hi_ready, B)
            pe.wait_ge(probs_ready, B - 2)
            product(last_s_ps[0], 0, score_terms(1), last_await_lo, part=range(2))
            product(early_w_ps[1], 1, value_terms(B - 3, 1)).then_inc(weighted_ready, 1)
            product(last_s_ps[0], 0, score_terms(1), last_await_lo, part=range(2, 3)).then_inc(last_scores, 1)
            transpose_p(B - 2, 0)
            product(last_s_ps[1], 1, score_terms(1)).then_inc(last_scores, 1)

            await_weigh(B - 2)
            await_lo = [(v_lo_ready, B - 1), (p_lo_ready, B - 1)]
            product(late_w_ps[0], 0, value_terms(B - 2, 0), await_lo, part=range(2))
            transpose_last(0)
            product(late_w_ps[1], 1, value_terms(B - 2, 0), part=range(2))
            product(late_w_ps[0], 0, value_terms(B - 2, 0), await_lo, part=range(2, 3)).then_inc(half_weighted, 1)
            transpose_last(1)
            product(late_w_ps[1], 1, value_terms(B - 2, 0), part=range(2, 3)).then_inc(weighted_ready, 1)
            for h in range(HALVES):
                pe.wait_ge(last_hi, h + 1)
                product(last_w_ps[h], h, value_terms(LAST, LAST % 2),
                        [(v_lo_ready, B), (last_lo, h + 1)]).then_inc(last_weighted, 1)


_INS = ["x", "fside_BxSxS_0", "itok_B_0_5", "L0_cond_braak_embed"]


def kernel(**inputs):
    import numpy as _np
    import concourse.bacc as _bacc
    from concourse import mybir as _mybir
    from concourse.bass_utils import run_bass_kernel_spmd as _run

    nc = _bacc.Bacc("TRN2", target_bir_lowering=False, num_devices=1)
    arrays, args = {}, []
    for name in _INS:
        a = _np.ascontiguousarray(inputs[name])
        arrays[f"in_{name}_dram"] = a
        args.append(nc.dram_tensor(f"in_{name}_dram", a.shape, _mybir.dt.from_np(a.dtype), kind="ExternalInput").ap())
    out = nc.dram_tensor("out_dram", inputs["x"].shape, _mybir.dt.float32, kind="ExternalOutput").ap()
    attention_with_stage_bias(nc, *args, out)
    r = _run(nc, [arrays], core_ids=[0])
    return r.results[0]["out_dram"]
```
